# Optimizing a Trainium2 kernel written in Bass

```python
import numpy as np
import jax
import jax.numpy as jnp

def _softmax(x, axis=-1):
    return jax.nn.softmax(x, axis=axis)

def _gelu(x):
    return jax.nn.gelu(x, approximate=True)

def _silu(x):
    return jax.nn.silu(x)

def _sigmoid(x):
    return jax.nn.sigmoid(x)

def _layernorm(x, axis=-1, eps=1e-05):
    m = jnp.mean(x, axis=axis, keepdims=True)
    v = jnp.var(x, axis=axis, keepdims=True)
    return (x - m) / jnp.sqrt(v + eps)

def _scatter_add(tgt, idx, src, axis=0):
    return tgt.at[idx].add(src)

def _segment_sum(src, seg, n):
    return jax.ops.segment_sum(src, seg, n)
kernel_name = 'mk_gnn_preln_d2_gnn_r8_7b07e5'

def setup_inputs(seed: int=0):
    np.random.seed(seed)
    _w = jnp.asarray

    def _rec_inputs():
        import jax
        import jax.numpy as jnp
        _gk = jax.random.key(seed)
        x = -0.0002928 + 1 * jax.random.normal(jax.random.fold_in(_gk, 1), (1024, 512), jnp.float32)
        src = jax.random.randint(jax.random.fold_in(_gk, 2), (32768,), 0, 1024, jnp.int32)
        dst = jax.random.randint(jax.random.fold_in(_gk, 3), (32768,), 0, 1024, jnp.int32)
        _o = jnp.argsort(dst, stable=True)
        src = src[_o]
        dst = dst[_o]
        edge_type_8 = jax.random.randint(jax.random.fold_in(_gk, 13), (32768,), 0, 8, jnp.int32)
        edge_weight = jax.random.uniform(jax.random.fold_in(_gk, 14), (32768,), jnp.float32, 0.0, 0.999998)
        return (x, src, dst, edge_type_8, edge_weight)
    x, src, dst, edge_type_8, edge_weight = _rec_inputs()

    def _L0_gnn_setup():
        import jax, jax.numpy as jnp
        import numpy as np
        N_NODES = 1024
        N_EDGES = 32768
        D_IN = 512
        D_OUT = 512
        key = jax.random.key(seed)
        k1, k2, k3 = jax.random.split(key, 3)
        x = jax.random.normal(k1, (N_NODES, D_IN), dtype=jnp.float32)
        edge_index = jax.random.randint(k2, (2, N_EDGES), 0, N_NODES, dtype=jnp.int64)
        weight = jax.random.normal(k3, (D_IN, D_OUT), dtype=jnp.float32)
        bias = jnp.zeros((D_OUT,), dtype=jnp.float32)
        return {'x': x, 'edge_index': edge_index, 'weight': weight, 'bias': bias}
    _L0_gnn_all = _L0_gnn_setup()
    _L0_gnn_in = {k: v for k, v in _L0_gnn_all.items() if k in ('weight', 'bias')}
    del _L0_gnn_all

    def _L1_gnn_setup():
        import jax, jax.numpy as jnp
        import numpy as np
        N_NODES = 2500
        N_EDGES = 40000
        D = 512
        NUM_RELS = 8
        NUM_BASES = 4

        def _rel_graph_conv(h, src, dst, etypes, norm, basis, comp, bias, loop_w, apply_relu):
            n = h.shape[0]
            hb = jnp.einsum('nd,bdo->bno', h, basis)
            coef = comp[etypes]
            m = coef[:, 0, None] * hb[0][src]
            for b in range(1, basis.shape[0]):
                m = m + coef[:, b, None] * hb[b][src]
            m = m * norm[:, None]
            agg = jax.ops.segment_sum(m, dst, num_segments=n)
            out = agg + bias + h @ loop_w
            if apply_relu:
                out = jax.nn.relu(out)
            return out
        key = jax.random.key(seed)
        ks = jax.random.split(key, 16)
        inp = {'emb': jax.random.normal(ks[0], (N_NODES, D), dtype=jnp.float32), 'src': jax.random.randint(ks[1], (N_EDGES,), 0, N_NODES), 'dst': jax.random.randint(ks[2], (N_EDGES,), 0, N_NODES), 'etypes': jax.random.randint(ks[3], (N_EDGES,), 0, NUM_RELS), 'edge_norm': jax.random.uniform(ks[4], (N_EDGES,), dtype=jnp.float32)}
        s = 1.0 / np.sqrt(D)
        inp['basis0'] = jax.random.normal(ks[5], (NUM_BASES, D, D), dtype=jnp.float32) * s
        inp['comp0'] = jax.random.normal(ks[6], (NUM_RELS, NUM_BASES), dtype=jnp.float32)
        inp['bias0'] = jnp.zeros((D,), dtype=jnp.float32)
        inp['loop0'] = jax.random.normal(ks[7], (D, D), dtype=jnp.float32) * s
        inp['basis1'] = jax.random.normal(ks[8], (NUM_BASES, D, D), dtype=jnp.float32) * s
        inp['comp1'] = jax.random.normal(ks[9], (NUM_RELS, NUM_BASES), dtype=jnp.float32)
        inp['bias1'] = jnp.zeros((D,), dtype=jnp.float32)
        inp['loop1'] = jax.random.normal(ks[10], (D, D), dtype=jnp.float32) * s
        return inp
    _L1_gnn_all = _L1_gnn_setup()
    _L1_gnn_in = {k: v for k, v in _L1_gnn_all.items() if k in ('basis0', 'comp0', 'bias0', 'loop0', 'basis1', 'comp1', 'bias1', 'loop1')}
    del _L1_gnn_all
    return {'x': x, 'src': src, 'dst': dst, 'edge_type_8': edge_type_8, 'edge_weight': edge_weight, 'L0_gnn_weight': _L0_gnn_in['weight'], 'L0_gnn_bias': _L0_gnn_in['bias'], 'L1_gnn_basis0': _L1_gnn_in['basis0'], 'L1_gnn_comp0': _L1_gnn_in['comp0'], 'L1_gnn_bias0': _L1_gnn_in['bias0'], 'L1_gnn_loop0': _L1_gnn_in['loop0'], 'L1_gnn_basis1': _L1_gnn_in['basis1'], 'L1_gnn_comp1': _L1_gnn_in['comp1'], 'L1_gnn_bias1': _L1_gnn_in['bias1'], 'L1_gnn_loop1': _L1_gnn_in['loop1']}

def reference(x, src, dst, edge_type_8, edge_weight, L0_gnn_weight, L0_gnn_bias, L1_gnn_basis0, L1_gnn_comp0, L1_gnn_bias0, L1_gnn_loop0, L1_gnn_basis1, L1_gnn_comp1, L1_gnn_bias1, L1_gnn_loop1):
    import jax
    import jax.numpy as jnp

    def _L0_gnn_ref(x, edge_index, weight, bias):
        import jax, jax.numpy as jnp
        import numpy as np
        N_NODES = 1024
        N_EDGES = 32768
        D_IN = 512
        D_OUT = 512
        n = x.shape[0]
        adj = jnp.zeros((n, n), dtype=x.dtype)
        adj = adj.at[edge_index[0], edge_index[1]].set(1.0)
        adj = adj.at[edge_index[1], edge_index[0]].set(1.0)
        adj = adj + jnp.eye(n, dtype=x.dtype)
        deg = jnp.sum(adj, axis=1)
        dinv = 1.0 / jnp.sqrt(deg)
        adj = adj * dinv[:, None] * dinv[None, :]
        return adj @ (x @ weight) + bias

    def _L1_gnn_ref(emb, src, dst, etypes, edge_norm, basis0, comp0, bias0, loop0, basis1, comp1, bias1, loop1):
        import jax, jax.numpy as jnp
        import numpy as np
        N_NODES = 2500
        N_EDGES = 40000
        D = 512
        NUM_RELS = 8
        NUM_BASES = 4

        def _rel_graph_conv(h, src, dst, etypes, norm, basis, comp, bias, loop_w, apply_relu):
            n = h.shape[0]
            hb = jnp.einsum('nd,bdo->bno', h, basis)
            coef = comp[etypes]
            m = coef[:, 0, None] * hb[0][src]
            for b in range(1, basis.shape[0]):
                m = m + coef[:, b, None] * hb[b][src]
            m = m * norm[:, None]
            agg = jax.ops.segment_sum(m, dst, num_segments=n)
            out = agg + bias + h @ loop_w
            if apply_relu:
                out = jax.nn.relu(out)
            return out
        h = _rel_graph_conv(emb, src, dst, etypes, edge_norm, basis0, comp0, bias0, loop0, True)
        h = _rel_graph_conv(h, src, dst, etypes, edge_norm, basis1, comp1, bias1, loop1, False)
        return h
    edge_index = jnp.stack([src, dst])
    h = jnp.maximum(_layernorm(x, axis=-1), 0.0)
    x = x + _L0_gnn_ref(h, edge_index, L0_gnn_weight, L0_gnn_bias)
    h = jnp.maximum(_layernorm(x, axis=-1), 0.0)
    x = x + _L1_gnn_ref(h, src, dst, edge_type_8, edge_weight, L1_gnn_basis0, L1_gnn_comp0, L1_gnn_bias0, L1_gnn_loop0, L1_gnn_basis1, L1_gnn_comp1, L1_gnn_bias1, L1_gnn_loop1)
    return x

_drawn_inputs = setup_inputs


def setup_inputs(seed=0):
    import zlib

    import numpy as np

    out = dict(_drawn_inputs(seed))
    spreads = {'L0_gnn_bias': (0.0, 0.8), 'L1_gnn_bias0': (0.0, 0.44), 'L1_gnn_bias1': (0.0, 2.0)}
    factors = {}
    for name, (base, spread) in spreads.items():
        noise = np.random.default_rng([zlib.crc32(name.encode()), seed]).standard_normal(out[name].shape)
        drawn = base * np.exp(spread * noise) if base else spread * noise
        out[name] = jnp.asarray(drawn.astype(out[name].dtype))
    for name, factor in factors.items():
        out[name] = (out[name] * factor).astype(out[name].dtype)
    return out
```

```python
from contextlib import ExitStack

import concourse.bass as bass
from concourse import mybir

ALU = mybir.AluOpType
ACT = mybir.ActivationFunctionType
AX_X = mybir.AxisListType.X
F32, F32R, BF16, F16, I32 = (mybir.dt.float32, mybir.dt.float32r, mybir.dt.bfloat16,
                             mybir.dt.float16, mybir.dt.int32)

P = 128
N, D, E = 1024, 512, 32768
RELS, BASES, LAYERS = 8, 4, 2
NB = N // P
KB = D // P
TILES = E // P
TC = TILES // P
MATS = LAYERS * BASES
PARTS = 3
W = 8
BINS = N // W
COLS = (MATS * PARTS + 1) * W
COUNT = MATS * PARTS * W
SB = 256
RING = 8
GB = P // W
GROUPS = BINS // GB
HALF = 512
HB = HALF // P
EPS = 1e-5
PASSES = ((0, 0), (0, 1), (1, 0))


def program(nc, x, src, dst, etype, weight, w0, b0, basis0, comp0, bias0, loop0,
            basis1, comp1, bias1, loop1, m_store, out, dbg=None):
    with ExitStack() as ctx:
        def sb(name, shape, dt, scope=ctx):
            return scope.enter_context(nc.sbuf_tensor(name, shape, dt))

        def sem(name):
            return ctx.enter_context(nc.semaphore(name))

        bias_x = sb("bias_x", [P, D + NB * D], F32)
        bias0_sb = bias_x[:, 0:D]
        x_sb = bias_x[:, D:].rearrange("p (n d) -> p n d", n=NB)
        ident = sb("ident", [P, P], F32)
        ident_r = sb("ident_r", [P, P], F32R)
        zeros16 = sb("zeros16", [P, P], BF16)
        ident16 = sb("ident16", [P, P], BF16)
        bias1_sb = sb("bias1_sb", [P, D], F32)
        stats = sb("stats", [P, NB, nc.vector.BN_STATS_DIM], F32)
        moments = sb("moments", [P, NB, nc.vector.BN_AGGR_DIM], F32)
        small = sb("small", [P, 8, NB], F32)

        first = ExitStack()
        xw = sb("xw", [P, NB, D], F32, first)
        counts = sb("counts", [P, NB, N], BF16, first)

        making = ExitStack()
        ones = sb("ones", [P, P], F32, making)
        iota_n = sb("iota_n", [P, N], F16, making)
        raw_i = sb("raw_i", [P, 3, TC, P], I32, making)
        raw_f = sb("raw_f", [P, 4, TC, P], F32, making)
        tile_min = sb("tile_min", [P, TC], F32, making)
        tile_max = sb("tile_max", [P, TC], F32, making)
        bin_lo = sb("bin_lo", [P, BINS], F32, making)
        bin_hi = sb("bin_hi", [P, BINS], F32, making)
        tile_no = sb("tile_no", [P, 2, TC], F32, making)
        above = sb("above", [P, TC, BINS], F32, making)
        cover = sb("cover", [P, TC, BINS], F32, making)
        visits = sb("visits", [P, 2, TC, BINS], F32, making)
        ends = sb("ends", [P, 4], F32, making)
        bounds = sb("bounds", [1, 2 * BINS], I32, making)
        per_edge = sb("per_edge", [P, 4, TILES], F32, making)
        comp_sb = sb("comp_sb", [P, LAYERS, RELS, BASES], F32, making)
        typed_w = sb("typed_w", [P, RELS, TILES], F32, making)
        coef_f = sb("coef_f", [P, MATS, TILES], F32, making)
        coef = sb("coef", [P, TILES, PARTS * MATS + 1], BF16, making)
        src_hot = sb("src_hot", [P, RING * N], BF16, making)
        dst_hot = sb("dst_hot", [P, RING * W], BF16, making)
        moving = sb("moving", [P, RING * COLS], BF16, making)
        w0_raw = sb("w0_raw", [P, KB, D], F32, making)
        grouping = ExitStack()
        m_group = sb("m_group", [P, 2 * MATS * N], F32, grouping)
        grouping.close()
        h0 = sb("h0", [P, NB, D], F32, making)
        h0t = sb("h0t", [P, 2, KB, N], F32R, making)
        w0_hl = sb("w0_hl", [P, 2, KB, D], F32R, making)
        making.close()

        adj = sb("adj", [P, NB, N], F32R, first)
        y_hl = sb("y_hl", [P, 2, NB, D], F32R, first)
        first.close()

        w_hl = sb("w_hl", [P, 2, KB, D], F32R)
        pt = sb("pt", [P, 2, 2, KB, HALF], F32R)
        m_hl1 = sb("m_hl1", [P, 2, HB, NB, P], F32R)
        w_raw = sb("w_raw", [P, KB, D], F32)
        sb("gap", [P, 2 * N], F32)
        h2 = sb("h2", [P, NB, D], F32)
        h_hl = sb("h_hl", [P, 2, NB, D], F32R)
        m_hl0 = sb("m_hl0", [P, 2, HB, NB, P], F32R)
        m_raw = sb("m_raw", [P, 2, N], F32)
        m_hl = [m_hl0, m_hl1]

        banks = ctx.enter_context(nc.psum_tensor("banks", [P, 8, 512], F32))
        acc = [banks[:, 4 * i:4 * i + 4, :].rearrange("p q (s c) -> p (q s) c", c=SB) for i in range(2)]
        banks16 = banks[:].bitcast(BF16)

        s_edges = [sem(f"edges_loaded{i}") for i in range(5)]
        s_const = sem("consts_made")
        s_cast = sem("edges_cast")
        s_turned = sem("edges_turned")
        s_per_edge = sem("per_edge_ready")
        s_minmax = sem("tile_range")
        s_above = sem("above_ready")
        s_cover = sem("cover_ready")
        s_visits = sem("visits_ready")
        s_vturn = sem("visits_turned")
        s_ends = sem("bin_ends")
        s_ends_row = sem("bin_ends_row")
        s_bounds = sem("bounds_ready")
        s_typed = sem("typed_weights")
        s_coef = sem("coef_steps")
        s_coef_ready = sem("coef_ready")
        s_free = sem("ring_free")
        s_src = sem("src_hot_ready")
        s_dsth = sem("dst_hot_ready")
        s_dstfree = sem("dst_hot_used")
        s_mov = sem("moving_ready")
        s_bin = sem("bin_summed")
        s_evac1 = sem("bin_first_part")
        s_evac2 = sem("bin_second_part")
        s_evac = sem("bin_out")
        s_cnt = sem("bin_counts_out")
        s_mfree = sem("group_free")
        s_stored = sem("group_stored")

        s_identr = sem("ident_r_made")
        s_x = sem("x_loaded")
        s_w0 = sem("w0_loaded")
        s_bias = [sem(f"bias{i}_loaded") for i in range(3)]
        s_bn = sem("ln_stats")
        s_mv = sem("ln_moments")
        s_eps = sem("ln_variance_plus_eps")
        s_sqrt = sem("ln_sqrt")
        s_newton = sem("ln_newton_steps")
        s_ln = sem("ln_scale_ready")
        s_h0 = sem("h0_ready")
        s_h0turn = sem("h0_turned")
        s_h0t_hi = sem("h0t_upper")
        s_h0t_lo = sem("h0t_lower")
        s_w0_hi = sem("w0_upper")
        s_w0_lo = sem("w0_lower")
        s_xw = sem("xw_summed")
        s_xw_out = sem("xw_out")
        s_xb = sem("x_plus_bias")
        s_ctr = sem("counts_turned")
        s_adj = sem("adj_ready")
        s_adji = sem("adj_plus_identity")
        s_deg = sem("degrees")
        s_degrt = sem("degree_sqrt")
        s_dsteps = sem("degree_steps")
        s_dinv = sem("dinv_ready")
        s_y_hi = sem("y_upper")
        s_y_lo = sem("y_lower")
        s_l0 = sem("l0_summed")
        s_x1 = sem("x1_ready")
        s_x1b = sem("x1_plus_bias")
        s_h = sem("h_ready")
        s_h_hi = sem("h_upper")
        s_h_lo = sem("h_lower")
        s_mraw = [sem(f"m_raw{i}_in") for i in range(2)]
        s_wraw = [sem(f"w_raw{i}_in") for i in range(KB)]
        s_m_hi = sem("m_upper")
        s_m_lo = sem("m_lower")
        s_w_hi = sem("w_upper")
        s_w_lo = sem("w_lower")
        s_w_used = sem("w_used")
        s_p = sem("p_summed")
        s_pt_hi = sem("pt_upper")
        s_pt_lo = sem("pt_lower")
        s_out = sem("out_stored")

        def grab(eng, b):
            lo = eng.value_load(bounds[0:1, bass.ds(b, 1)], min_val=0, max_val=TILES - 1)
            hi = eng.value_load(bounds[0:1, bass.ds(b + BINS, 1)], min_val=1, max_val=TILES)
            return lo, hi

        def m_view(t, col):
            v = t[:, bass.ds(col, (MATS * NB - 1) * P + W)]
            return bass.AP(v.tensor, v.offset, [list(v.ap[0]), [P, NB], [N, MATS], [1, W]])

        def last_or_bias(eng, l, n):
            return bias_x[:, bass.ds(l * (D + n * D), D)]

        def counter(eng, name):
            r = eng.alloc_register(name)
            eng.reg_mov(r, 0)
            return r

        def current(eng, r, top=TILES * BINS):
            return eng.snap(r, min_val=0, max_val=top)

        block = ctx.enter_context(nc.Block())

        @block.sync
        def _(sp):
            for i, a in enumerate((dst, src, etype)):
                sp.dma_start(raw_i[:, i], a.rearrange("(c p e) -> p c e", p=P, e=P)).then_inc(s_edges[i], 16)
            sp.dma_start(x_sb, x.rearrange("(n p) d -> p n d", p=P)).then_inc(s_x, 16)
            sp.dma_start(raw_f[:, 3], weight.rearrange("(c p e) -> p c e", p=P, e=P)).then_inc(s_edges[3], 16)
            for l, a in enumerate((comp0, comp1)):
                sp.dma_start(comp_sb[:, l].rearrange("p r b -> p (r b)"),
                             a.rearrange("r b -> (r b)").partition_broadcast(P)).then_inc(s_edges[4], 16)
            sp.dma_start(w0_raw[:], w0.rearrange("(k p) d -> p k d", p=P)).then_inc(s_w0, 16)
            sp.dma_start(bias0_sb, b0.partition_broadcast(P)).then_inc(s_bias[0], 16)
            sp.sem_inc(s_m_lo, 2)
            sp.sem_inc(s_mfree, 2)
            for g in range(GROUPS):
                sp.wait_ge(s_evac, GB * (g + 1) + 2)
                sp.dma_start(m_store[g].rearrange("m p n -> p m n"),
                             m_group[:, (g % 2) * MATS * N:(g % 2 + 1) * MATS * N].rearrange("p (m n) -> p m n", m=MATS)
                             ).then_inc(s_stored, 16)
                sp.wait_ge(s_stored, 16 * (g + 1))
                sp.sem_inc(s_mfree, 1)
            sp.wait_ge(s_stored, 16 * GROUPS)
            sp.wait_ge(s_free, RING)
            with sp.Fori(0, LAYERS) as l, sp.Fori(0, 2) as half, sp.Fori(0, BASES) as base:
                unit = sp.snap((l * 2 + half) * BASES + base)
                first_chunk = sp.snap(half * (HB * MATS * P * N) + (l * BASES + base) * (P * N))
                for j in range(HB):
                    chunk = sp.snap(first_chunk + j * (MATS * P * N))
                    sp.wait_ge(s_m_lo, unit * HB + j + 1)
                    sp.dma_start(m_raw[:, j % 2], bass.AP(m_store.tensor, chunk, [[N, P], [1, N]])
                                 ).then_inc(s_mraw[j % 2], 16)
            for n in range(NB):
                sp.wait_ge(s_h, NB * LAYERS + n + 1)
                sp.dma_start(out[n * P:(n + 1) * P], h2[:, n]).then_inc(s_out, 16)
            sp.wait_ge(s_out, 16 * NB)

        @block.gpsimd
        def _(pool):
            pool.memset(ones[:], 1.0).then_inc(s_const, 1)
            pool.memset(zeros16[:], 0.0).then_inc(s_const, 1)
            pool.iota(iota_n[:], [[1, N]], base=0, channel_multiplier=0,
                      allow_small_or_imprecise_dtypes=True).then_inc(s_const, 1)
            pool.iota(bin_lo[:], [[W, BINS]], base=0, channel_multiplier=0,
                      allow_small_or_imprecise_dtypes=True).then_inc(s_const, 1)
            pool.iota(bin_hi[:], [[W, BINS]], base=W - 1, channel_multiplier=0,
                      allow_small_or_imprecise_dtypes=True).then_inc(s_const, 1)
            pool.iota(tile_no[:, 0], [[P, TC]], base=1, channel_multiplier=1,
                      allow_small_or_imprecise_dtypes=True).then_inc(s_const, 1)
            pool.iota(tile_no[:, 1], [[-P, TC]], base=TILES, channel_multiplier=-1,
                      allow_small_or_imprecise_dtypes=True).then_inc(s_const, 1)
            pool.wait_ge(s_const, 1)
            pool.affine_select(out=ident[:], in_=ones[:], compare_op=ALU.is_equal, fill=0.0, base=0,
                               pattern=[[-1, P]], channel_multiplier=1).then_inc(s_const, 1)
            pool.wait_ge(s_const, 8)
            pool.tensor_copy(ident16[:], ident[:]).then_inc(s_const, 1)
            pool.memset(coef[:, :, PARTS * MATS:], 1.0).then_inc(s_const, 1)
            pool.wait_ge(s_bias[0], 16)
            pool.wait_ge(s_h0, NB)
            for n in range(NB):
                pool.tensor_tensor(x_sb[:, n], x_sb[:, n], bias0_sb, ALU.add).then_inc(s_xb, 1)
            k = counter(pool, "pool_item")
            pool.wait_ge(s_coef_ready, 3)
            pool.wait_ge(s_const, 10)
            pool.wait_ge(s_bounds, 1)
            with pool.Fori(0, BINS) as b:
                lo, hi = grab(pool, b)
                with pool.Fori(lo, hi) as t:
                    i = current(pool, k)
                    slot = pool.snap(i % RING)
                    pool.wait_ge(s_dsth, i + 1)
                    pool.tensor_tensor(
                        moving[:, bass.ds(slot * COLS, COLS)].rearrange("p (j w) -> p j w", w=W),
                        coef[:, bass.ds(t, 1), :].rearrange("p a j -> p (a j)").unsqueeze(2).broadcast_to([P, PARTS * MATS + 1, W]),
                        dst_hot[:, bass.ds(slot * W, W)].unsqueeze(1).broadcast_to([P, PARTS * MATS + 1, W]),
                        ALU.mult).then_inc(s_mov, 1)
                    pool.reg_add(k, k, 1)

            pool.wait_ge(s_xb, NB)
            pool.dma_start(bias0_sb, bias0.partition_broadcast(P)).then_inc(s_bias[1], 16)
            pool.dma_start(bias1_sb[:], bias1.partition_broadcast(P)).then_inc(s_bias[2], 16)
            pool.wait_ge(s_bias[2], 16)
            pool.wait_ge(s_h, NB)
            for n in range(NB):
                pool.tensor_tensor(x_sb[:, n], x_sb[:, n], bias1_sb[:], ALU.add).then_inc(s_x1b, 1)
            pool.sem_inc(s_w_lo, KB)
            for l, (basis, loop) in enumerate(((basis0, loop0), (basis1, loop1))):
                for dh in range(2):
                    for u in range(BASES + 1):
                        for k in range(KB):
                            src_rows = (loop if u == 0 else basis[u - 1])[k * P:(k + 1) * P]
                            pool.wait_ge(s_w_lo, ((2 * l + dh) * (BASES + 1) + u) * KB + k + 1)
                            pool.dma_start(w_raw[:, k], src_rows).then_inc(s_wraw[k], 16)

        @block.scalar
        def _(act):
            for i in range(4):
                act.wait_ge(s_turned, TC * (i + 1))
                nc.scalar.copy(per_edge[:, i].rearrange("p (c t) -> p c t", c=TC),
                               acc[0][:, 2 * i, 0:TC * P].rearrange("p (c t) -> p c t", c=TC)).then_inc(s_per_edge, 1)
            act.wait_ge(s_eps, 1)
            nc.scalar.activation(small[:, 1], small[:, 0], ACT.Sqrt).then_inc(s_sqrt, 1)
            act.wait_ge(s_w0, 16)
            nc.scalar.copy(w0_hl[:, 0], w0_raw[:]).then_inc(s_w0_hi, 1)
            act.wait_ge(s_ln, 1)
            for n in range(NB):
                nc.scalar.activation(h0[:, n], x_sb[:, n], ACT.Relu, bias=small[:, 5, n:n + 1],
                                     scale=small[:, 4, n:n + 1]).then_inc(s_h0, 1)
            for i in range(2 * KB):
                act.wait_ge(s_h0turn, i + 1)
                nc.scalar.copy(h0t[:, 0, i // 2, (i % 2) * HALF:(i % 2 + 1) * HALF], banks[:, 6 + i % 2]).then_inc(s_h0t_hi, 1)
            for n in range(NB):
                act.wait_ge(s_xw, n + 1)
                nc.scalar.copy(xw[:, n], banks[:, 6 + n % 2]).then_inc(s_xw_out, 1)
            with act.Fori(0, BINS // 2) as bb:
                for half in range(2):
                    b = act.snap(bb * 2 + half)
                    col = act.snap(((b >> 4) & 1) * (MATS * N) + (b & (GB - 1)) * W)
                    act.wait_ge(s_bin, b + 1)
                    act.wait_ge(s_mfree, (b >> 4) + 1)
                    nc.scalar.activation(counts[:, :, bass.ds(b * W, W)], acc[half][:, :, COUNT:COUNT + W],
                                         ACT.Sign).then_inc(s_cnt, 1)
                    nc.scalar.copy(
                        m_view(m_group, col),
                        acc[half][:, :, 0:MATS * W].rearrange("p s (m w) -> p s m w", w=W)).then_inc(s_evac1, 1)

            for r in range(NB):
                act.wait_ge(s_adji, r + 1)
                nc.scalar.activation(y_hl[:, r // 4, r % 4 * 2:r % 4 * 2 + 2].rearrange("p a d -> p (a d)"), adj[:, r].bitcast(F32), ACT.Copy,
                                     accum_out=small[:, 0, r:r + 1]).then_inc(s_deg, 1)
            act.wait_ge(s_deg, NB)
            nc.scalar.activation(small[:, 1], small[:, 0], ACT.Sqrt).then_inc(s_degrt, 1)
            act.wait_ge(s_dinv, 1)
            for n in range(NB):
                nc.scalar.activation(y_hl[:, 0, n], xw[:, n], ACT.Copy, scale=small[:, 6, n:n + 1]).then_inc(s_y_hi, 1)
            act.wait_ge(s_eps, 2)
            nc.scalar.activation(small[:, 1], small[:, 0], ACT.Sqrt).then_inc(s_sqrt, 1)
            act.wait_ge(s_ln, 2)
            act.wait_ge(s_stored, 16 * GROUPS)
            for n in range(NB):
                nc.scalar.activation(h2[:, n], x_sb[:, n], ACT.Identity, bias=small[:, 5, n:n + 1],
                                     scale=small[:, 4, n:n + 1]).then_inc(s_h, 1)

            def upper_m(unit, slot, k):
                act.wait_ge(s_mraw[k % 2], (unit * 2 + k // 2 + 1) * 16)
                nc.scalar.copy(m_hl[slot][:, 0, k].rearrange("p s d -> p (s d)"), m_raw[:, k % 2]).then_inc(s_m_hi, 1)

            def upper_w(at, k):
                act.wait_ge(s_wraw[k], at * 4 + 16)
                act.wait_ge(s_w_used, at + k + 1)
                nc.scalar.copy(w_hl[:, 0, k], w_raw[:, k]).then_inc(s_w_hi, 1)

            def upper_p(at, u, k):
                act.wait_ge(s_p, at + k + 1)
                if k == 0:
                    act.wait_ge(s_w_used, at - KB * min(u, 1) + KB)
                nc.scalar.copy(pt[:, u % 2, 0, k], banks[:, k]).then_inc(s_pt_hi, 1)

            with act.Fori(0, LAYERS) as l:
                for n in range(NB):
                    act.wait_ge(s_h, l * NB + n + 1)
                    nc.scalar.activation(h_hl[:, 0, n], h2[:, n], ACT.Relu).then_inc(s_h_hi, 1)
                for dh in range(2):
                    at = [act.snap(l * (2 * (BASES + 1) * KB) + (dh * (BASES + 1) + u) * KB) for u in range(BASES + 1)]
                    unit = [act.snap(l * (2 * BASES) + dh * BASES + u) for u in range(BASES)]
                    for k in range(HB):
                        upper_m(unit[0], 0, k)
                    for k in range(KB):
                        upper_p(at[0], 0, k)
                    for u in range(1, BASES + 1):
                        for k in range(KB):
                            upper_w(at[u - 1], k)
                        for k in range(KB):
                            if u < BASES:
                                upper_m(unit[u], u % 2, k)
                            upper_p(at[u], u, k)
                    for k in range(KB):
                        upper_w(at[BASES], k)

        @block.vector
        def _(dve):
            def root_steps(count, done):
                nc.vector.reciprocal(small[:, 2], small[:, 1]).then_inc(done, 1)
                dve.wait_ge(done, count + 1)
                nc.vector.tensor_tensor(small[:, 2], small[:, 0], small[:, 2], ALU.mult).then_inc(done, 1)
                dve.wait_ge(done, count + 2)
                nc.vector.tensor_tensor(small[:, 2], small[:, 2], small[:, 1], ALU.add).then_inc(done, 1)
                dve.wait_ge(done, count + 3)
                nc.vector.tensor_scalar(small[:, 2], small[:, 2], 0.5, None, ALU.mult).then_inc(done, 1)
                dve.wait_ge(done, count + 4)

            def normalise(i):
                dve.wait_ge(s_bn, NB * (i + 1))
                for n in range(NB):
                    nc.vector.bn_aggr(moments[:, n], stats[:, n]).then_inc(s_mv, 1)
                dve.wait_ge(s_mv, NB * (i + 1))
                nc.vector.tensor_scalar(small[:, 0], moments[:, :, 1], EPS, None, ALU.add).then_inc(s_eps, 1)
                dve.wait_ge(s_eps, i + 1)
                dve.wait_ge(s_sqrt, i + 1)
                root_steps(5 * i, s_newton)
                nc.vector.reciprocal(small[:, 4], small[:, 2]).then_inc(s_newton, 1)
                dve.wait_ge(s_newton, 5 * i + 5)
                nc.vector.scalar_tensor_tensor(out=small[:, 5], in0=moments[:, :, 0], scalar=-1.0, in1=small[:, 4],
                                               op0=ALU.mult, op1=ALU.mult).then_inc(s_ln, 1)

            dve.wait_ge(s_const, 8)
            nc.vector.tensor_copy(ident_r[:], ident[:]).then_inc(s_identr, 1)
            for i in range(3):
                dve.wait_ge(s_edges[i], 16)
                nc.vector.tensor_copy(raw_f[:, i], raw_i[:, i]).then_inc(s_cast, 1)
            dve.wait_ge(s_cast, 1)
            nc.vector.tensor_reduce(tile_min[:], raw_f[:, 0], AX_X, ALU.min).then_inc(s_minmax, 1)
            nc.vector.tensor_reduce(tile_max[:], raw_f[:, 0], AX_X, ALU.max).then_inc(s_minmax, 1)
            dve.wait_ge(s_minmax, 2)
            dve.wait_ge(s_const, 7)
            for c in range(TC):
                nc.vector.tensor_scalar(above[:, c], bin_hi[:], tile_min[:, c:c + 1], None,
                                        ALU.is_ge).then_inc(s_above, 1)
            dve.wait_ge(s_above, TC)
            for c in range(TC):
                nc.vector.scalar_tensor_tensor(out=cover[:, c], in0=bin_lo[:], scalar=tile_max[:, c:c + 1],
                                               in1=above[:, c], op0=ALU.is_le, op1=ALU.mult).then_inc(s_cover, 1)
            dve.wait_ge(s_cover, TC)
            for c in range(TC):
                for j in range(2):
                    nc.vector.tensor_scalar(visits[:, j, c], cover[:, c], tile_no[:, j, c:c + 1], None,
                                            ALU.mult).then_inc(s_visits, 1)
            dve.wait_ge(s_vturn, 4)
            nc.vector.tensor_reduce(ends[:, 2:4], acc[1][:, 0:2, 0:TC * P], AX_X, ALU.max).then_inc(s_ends, 1)
            dve.wait_ge(s_ends, 1)
            nc.vector.tensor_scalar(ends[:, 1:2], ends[:, 2:3], 1.0, None, ALU.max).then_inc(s_ends, 1)
            nc.vector.tensor_scalar(ends[:, 3:4], ends[:, 3:4], -1.0, float(TILES), ALU.mult,
                                    ALU.add).then_inc(s_ends, 1)
            dve.wait_ge(s_ends, 3)
            nc.vector.scalar_tensor_tensor(out=ends[:, 0:1], in0=ends[:, 1:2], scalar=-1.0, in1=ends[:, 3:4],
                                           op0=ALU.add, op1=ALU.min).then_inc(s_ends, 1)
            dve.wait_ge(s_ends_row, 1)
            nc.vector.tensor_copy(bounds[:], acc[1][0:1, 2, 0:2 * BINS]).then_inc(s_bounds, 1)
            dve.wait_ge(s_x, 16)
            for n in range(NB):
                nc.vector.bn_stats(stats[:, n], x_sb[:, n]).then_inc(s_bn, 1)
            normalise(0)
            dve.wait_ge(s_w0_hi, 1)
            nc.vector.tensor_tensor(w0_hl[:, 1], w0_raw[:], w0_hl[:, 0].bitcast(F32), ALU.subtract).then_inc(s_w0_lo, 1)
            for i in range(2 * KB):
                dve.wait_ge(s_h0t_hi, i + 1)
                c = slice((i % 2) * HALF, (i % 2 + 1) * HALF)
                nc.vector.tensor_tensor(h0t[:, 1, i // 2, c], banks[:, 6 + i % 2], h0t[:, 0, i // 2, c].bitcast(F32),
                                        ALU.subtract).then_inc(s_h0t_lo, 1)
            dve.wait_ge(s_per_edge, 4)
            for r in range(RELS):
                nc.vector.scalar_tensor_tensor(out=typed_w[:, r], in0=per_edge[:, 2], scalar=float(r),
                                               in1=per_edge[:, 3], op0=ALU.is_equal, op1=ALU.mult).then_inc(s_typed, 1)
            dve.wait_ge(s_typed, RELS)
            dve.wait_ge(s_edges[4], 32)
            for r in range(RELS):
                if r:
                    dve.wait_ge(s_coef, MATS * r)
                for m in range(MATS):
                    scale = comp_sb[:, m // BASES, r, m % BASES:m % BASES + 1]
                    if r == 0:
                        nc.vector.tensor_scalar(coef_f[:, m], typed_w[:, r], scale, None, ALU.mult).then_inc(s_coef, 1)
                    else:
                        nc.vector.scalar_tensor_tensor(out=coef_f[:, m], in0=typed_w[:, r], scalar=scale,
                                                       in1=coef_f[:, m], op0=ALU.mult, op1=ALU.add).then_inc(s_coef, 1)
            dve.wait_ge(s_coef, MATS * RELS)
            for part in range(PARTS):
                view = coef[:, :, part * MATS:(part + 1) * MATS].rearrange("p t m -> p m t")
                nc.vector.tensor_copy(view, coef_f[:]).then_inc(s_coef_ready, 1)
                dve.wait_ge(s_coef_ready, part + 1)
                if part < PARTS - 1:
                    nc.vector.tensor_tensor(coef_f[:], coef_f[:], view, ALU.subtract).then_inc(s_coef, 1)
                    dve.wait_ge(s_coef, MATS * RELS + part + 1)

            k = counter(dve, "dve_item")

            def items(b):
                lo, hi = grab(dve, b)
                with dve.Fori(lo, hi) as t:
                    i = current(dve, k)
                    slot = dve.snap(i % RING)
                    dve.wait_ge(s_free, i + 1)
                    nc.vector.tensor_scalar(dst_hot[:, bass.ds(slot * W, W)], iota_n[:, bass.ds(b * W, W)],
                                            per_edge[:, 0, bass.ds(t, 1)], None, ALU.is_equal).then_inc(s_dsth, 1)
                    nc.vector.tensor_scalar(src_hot[:, bass.ds(slot * N, N)], iota_n[:],
                                            per_edge[:, 1, bass.ds(t, 1)], None, ALU.is_equal).then_inc(s_src, 1)
                    dve.reg_add(k, k, 1)

            def add_parts(b, half):
                col = dve.snap(((b >> 4) & 1) * (MATS * N) + (b & (GB - 1)) * W)
                for part, ready, done in ((1, s_evac1, s_evac2), (2, s_evac2, s_evac)):
                    dve.wait_ge(ready, b + 1)
                    v = m_view(m_group, col)
                    nc.vector.tensor_tensor(
                        v, v, acc[half][:, :, part * MATS * W:(part + 1) * MATS * W].rearrange("p s (m w) -> p s m w", w=W),
                        ALU.add).then_inc(done, 1)

            items(0)
            with dve.Fori(0, BINS // 2 - 1) as bb:
                for half in range(2):
                    b = dve.snap(bb * 2 + half)
                    items(dve.snap(b + 1))
                    add_parts(b, half)
            items(BINS - 1)
            add_parts(BINS - 2, 0)
            add_parts(BINS - 1, 1)

            for r in range(NB):
                dve.wait_ge(s_ctr, r + 1)
                nc.vector.tensor_tensor(adj[:, r], banks16[:, r], counts[:, r], ALU.max).then_inc(s_adj, 1)
                dve.wait_ge(s_adj, r + 1)
                diag = adj[:, r, r * P:(r + 1) * P]
                nc.vector.tensor_tensor(diag, diag.bitcast(F32), ident[:], ALU.add).then_inc(s_adji, 1)
            dve.wait_ge(s_degrt, 1)
            root_steps(0, s_dsteps)
            nc.vector.reciprocal(small[:, 6], small[:, 2]).then_inc(s_dinv, 1)
            dve.wait_ge(s_dinv, 1)
            for n in range(NB):
                dve.wait_ge(s_y_hi, n + 1)
                nc.vector.scalar_tensor_tensor(out=y_hl[:, 1, n], in0=xw[:, n], scalar=small[:, 6, n:n + 1],
                                               in1=y_hl[:, 0, n].bitcast(F32), op0=ALU.mult,
                                               op1=ALU.subtract).then_inc(s_y_lo, 1)
            dve.wait_ge(s_xb, NB)
            for n in range(NB):
                dve.wait_ge(s_l0, n + 1)
                nc.vector.scalar_tensor_tensor(out=x_sb[:, n], in0=banks[:, n], scalar=small[:, 6, n:n + 1],
                                               in1=x_sb[:, n], op0=ALU.mult, op1=ALU.add).then_inc(s_x1, 1)
                dve.wait_ge(s_x1, n + 1)
                nc.vector.bn_stats(stats[:, n], x_sb[:, n]).then_inc(s_bn, 1)
            normalise(1)

            def lower_m(unit, slot, k):
                dve.wait_ge(s_m_hi, unit * HB + k + 1)
                nc.vector.tensor_tensor(m_hl[slot][:, 1, k].rearrange("p s d -> p (s d)"), m_raw[:, k % 2],
                                        m_hl[slot][:, 0, k].bitcast(F32).rearrange("p s d -> p (s d)"),
                                        ALU.subtract).then_inc(s_m_lo, 1)

            def lower_w(at, k):
                dve.wait_ge(s_w_hi, at + k + 1)
                nc.vector.tensor_tensor(w_hl[:, 1, k], w_raw[:, k], w_hl[:, 0, k].bitcast(F32),
                                        ALU.subtract).then_inc(s_w_lo, 1)

            def lower_p(at, u, k):
                dve.wait_ge(s_pt_hi, at + k + 1)
                nc.vector.tensor_tensor(pt[:, u % 2, 1, k], banks[:, k], pt[:, u % 2, 0, k].bitcast(F32),
                                        ALU.subtract).then_inc(s_pt_lo, 1)

            def finish(l, dh):
                dve.wait_ge(s_w_used, KB + (l * 2 + dh + 1) * ((BASES + 1) * KB))
                for j in range(HB):
                    nc.vector.tensor_tensor(h2[:, dh * HB + j], banks[:, 4 + j],
                                            added[dh * HB + j], ALU.add).then_inc(s_h, 1)

            dve.wait_ge(s_bias[1], 16)
            dve.wait_ge(s_x1b, NB)
            with dve.Fori(0, LAYERS) as l:
                for n in range(NB):
                    dve.wait_ge(s_h_hi, l * NB + n + 1)
                    nc.vector.scalar_tensor_tensor(out=h_hl[:, 1, n], in0=h2[:, n], scalar=0.0,
                                                   in1=h_hl[:, 0, n].bitcast(F32), op0=ALU.max,
                                                   op1=ALU.subtract).then_inc(s_h_lo, 1)
                added = [last_or_bias(dve, l, n) for n in range(NB)]
                for dh in range(2):
                    at = [dve.snap(l * (2 * (BASES + 1) * KB) + (dh * (BASES + 1) + u) * KB) for u in range(BASES + 1)]
                    unit = [dve.snap(l * (2 * BASES) + dh * BASES + u) for u in range(BASES)]
                    for k in range(HB):
                        lower_m(unit[0], 0, k)
                    if dh == 1:
                        finish(l, 0)
                    for k in range(KB):
                        lower_p(at[0], 0, k)
                    for u in range(1, BASES + 1):
                        for k in range(KB):
                            lower_w(at[u - 1], k)
                        for k in range(KB):
                            if u < BASES:
                                lower_m(unit[u], u % 2, k)
                            lower_p(at[u], u, k)
                    for k in range(KB):
                        lower_w(at[BASES], k)
                finish(l, 1)

        @block.tensor
        def _(pe):
            pe.wait_ge(s_const, 8)
            for i in (0, 1, 2, 3):
                if i < 3:
                    pe.wait_ge(s_cast, i + 1)
                else:
                    pe.wait_ge(s_edges[3], 16)
                for c in range(TC):
                    pe.transpose(acc[0][:, 2 * i, c * P:(c + 1) * P], raw_f[:, i, c], ident[:]).then_inc(s_turned, 1)
            pe.wait_ge(s_visits, 2 * TC)
            for j in range(2):
                for c in range(TC):
                    pe.transpose(acc[1][:, j, c * P:(c + 1) * P], visits[:, j, c], ident[:]).then_inc(s_vturn, 1)
            pe.wait_ge(s_ends, 4)
            for j in range(2):
                last = pe.matmul(acc[1][0:1, 2, j * BINS:(j + 1) * BINS], ends[:, j:j + 1], ident[:],
                                 start=True, stop=True)
            last.then_inc(s_ends_row, 1)
            for i in range(2 * KB):
                pe.wait_ge(s_h0, NB // 2 * (i % 2 + 1))
                if i >= 2:
                    pe.wait_ge(s_h0t_lo, i - 1)
                for j in range(HB):
                    last = pe.transpose(banks[:, 6 + i % 2, j * P:(j + 1) * P],
                                        h0[:, (i % 2) * HB + j, (i // 2) * P:(i // 2 + 1) * P], ident[:])
                last.then_inc(s_h0turn, 1)
            pe.wait_ge(s_w0_lo, 1)
            pe.wait_ge(s_h0t_lo, 2 * KB)
            for n in range(NB):
                if n >= 2:
                    pe.wait_ge(s_xw_out, n - 1)
                for k in range(KB):
                    for a, b in PASSES:
                        last = pe.matmul(banks[:, 6 + n % 2], h0t[:, a, k, n * P:(n + 1) * P], w0_hl[:, b, k],
                                         start=(k == 0 and (a, b) == PASSES[0]), stop=(k == KB - 1 and (a, b) == PASSES[-1]))
                last.then_inc(s_xw, 1)
            pe.wait_ge(s_xw_out, NB)
            pe.sem_inc(s_free, RING)
            pe.sem_inc(s_evac, 2)
            pe.wait_ge(s_per_edge, 4)
            pe.wait_ge(s_bounds, 1)
            k = counter(pe, "pe_item")

            with pe.Fori(0, BINS // 2) as bb:
                for half in range(2):
                    b = pe.snap(bb * 2 + half)
                    lo, hi = grab(pe, b)
                    pe.wait_ge(s_evac, b + 1)
                    for q in range(NB // 2):
                        pe.matmul(acc[half][:, 2 * q, 0:2], zeros16[:], zeros16[:, 0:2], start=True, stop=True,
                                  skip_group_check=True)
                    with pe.Fori(lo, hi) as t:
                        i = current(pe, k)
                        slot = pe.snap(i % RING)
                        pe.wait_ge(s_mov, i + 1)
                        pe.wait_ge(s_src, i + 1)
                        for s in range(NB):
                            last = pe.matmul(acc[half][:, s, 0:COLS], src_hot[:, bass.ds(slot * N + s * P, P)],
                                             moving[:, bass.ds(slot * COLS, COLS)], start=False, stop=True,
                                             skip_group_check=True)
                        last.then_inc(s_free, 1)
                        pe.reg_add(k, k, 1)
                    pe.matmul(acc[half][:, 0, 0:2], zeros16[:], zeros16[:, 0:2], start=False, stop=True,
                              skip_group_check=True).then_inc(s_bin, 1)

            pe.wait_ge(s_evac, BINS + 2)
            pe.wait_ge(s_const, 10)
            for r in range(NB):
                for c in range(NB):
                    last = pe.transpose(banks16[:, r, c * P:(c + 1) * P], counts[:, c, r * P:(r + 1) * P], ident16[:])
                last.then_inc(s_ctr, 1)
            pe.wait_ge(s_y_lo, NB)
            for n in range(NB):
                for j in range(NB):
                    for a in range(2):
                        last = pe.matmul(banks[:, n], adj[:, j, n * P:(n + 1) * P], y_hl[:, a, j],
                                         start=(j == 0 and a == 0), stop=(j == NB - 1 and a == 1))
                last.then_inc(s_l0, 1)

            pe.wait_ge(s_identr, 1)
            pe.sem_inc(s_w_used, KB)
            pe.sem_inc(s_pt_lo, KB)

            def p_self(l, at, dh):
                for k in range(KB):
                    pe.wait_ge(s_pt_lo, at + k + 1)
                    for j in range(HB):
                        if k == 0:
                            pe.wait_ge(s_h_lo, l * NB + dh * HB + j + 1)
                        for a in range(2):
                            last = pe.matmul(banks[:, k, j * P:(j + 1) * P], h_hl[:, a, dh * HB + j, k * P:(k + 1) * P],
                                             ident_r[:], start=(a == 0), stop=(a == 1))
                    last.then_inc(s_p, 1)

            def p_base(l, at, unit, slot):
                pe.wait_ge(s_h_lo, l * NB + NB)
                pe.wait_ge(s_m_lo, unit * HB + HB + 2)
                for k in range(KB):
                    pe.wait_ge(s_pt_lo, at + k + 1)
                    for s in range(NB):
                        for a, b in PASSES:
                            last = pe.matmul(banks[:, k], h_hl[:, a, s, k * P:(k + 1) * P], m_hl[slot][:, b, :, s],
                                             start=(s == 0 and (a, b) == PASSES[0]),
                                             stop=(s == NB - 1 and (a, b) == PASSES[-1]))
                    last.then_inc(s_p, 1)

            def out_base(l, at, dh, u):
                if u == 0:
                    pe.wait_ge(s_h, l * NB + NB + dh * HB)
                pe.wait_ge(s_pt_lo, at + 2 * KB)
                for k in range(KB):
                    pe.wait_ge(s_w_lo, at + KB + k + 1)
                    for j in range(HB):
                        for a, b in PASSES:
                            last = pe.matmul(banks[:, 4 + j], pt[:, u % 2, a, k, j * P:(j + 1) * P], w_hl[:, b, k],
                                             start=(u == 0 and k == 0 and (a, b) == PASSES[0]),
                                             stop=(u == BASES and k == KB - 1 and (a, b) == PASSES[-1]))
                    last.then_inc(s_w_used, 1)

            with pe.Fori(0, LAYERS) as l:
                for dh in range(2):
                    at = [pe.snap(l * (2 * (BASES + 1) * KB) + (dh * (BASES + 1) + u) * KB) for u in range(BASES + 1)]
                    unit = [pe.snap(l * (2 * BASES) + dh * BASES + u) for u in range(BASES)]
                    p_self(l, at[0], dh)
                    for u in range(1, BASES + 1):
                        p_base(l, at[u], unit[u - 1], (u - 1) % 2)
                        out_base(l, at[u - 1], dh, u - 1)
                    out_base(l, at[BASES], dh, BASES)


_INS = ["x", "src", "dst", "edge_type_8", "edge_weight", "L0_gnn_weight", "L0_gnn_bias",
        "L1_gnn_basis0", "L1_gnn_comp0", "L1_gnn_bias0", "L1_gnn_loop0",
        "L1_gnn_basis1", "L1_gnn_comp1", "L1_gnn_bias1", "L1_gnn_loop1"]


def kernel(**inputs):
    import numpy as np
    import concourse.bacc as bacc
    from concourse.bass_utils import run_bass_kernel_spmd

    nc = bacc.Bacc("TRN2", target_bir_lowering=False, num_devices=1)
    arrays, args = {}, []
    for name in _INS:
        a = np.ascontiguousarray(inputs[name])
        arrays[f"in_{name}"] = a
        args.append(nc.dram_tensor(f"in_{name}", a.shape, mybir.dt.from_np(a.dtype), kind="ExternalInput").ap())
    m_store = nc.dram_tensor("m_store", (GROUPS, MATS, P, N), F32, kind="Internal").ap()
    out = nc.dram_tensor("out", (N, D), F32, kind="ExternalOutput").ap()
    program(nc, *args, m_store, out)
    r = run_bass_kernel_spmd(nc, [arrays], core_ids=[0])
    return r.results[0]["out"]
```
